# Optimizing a Trainium2 kernel written in Bass

```python
import numpy as np
import jax
import jax.numpy as jnp

def _softmax(x, axis=-1):
    return jax.nn.softmax(x, axis=axis)

def _gelu(x):
    return jax.nn.gelu(x, approximate=True)

def _silu(x):
    return jax.nn.silu(x)

def _sigmoid(x):
    return jax.nn.sigmoid(x)

def _layernorm(x, axis=-1, eps=1e-05):
    m = jnp.mean(x, axis=axis, keepdims=True)
    v = jnp.var(x, axis=axis, keepdims=True)
    return (x - m) / jnp.sqrt(v + eps)

def _scatter_add(tgt, idx, src, axis=0):
    return tgt.at[idx].add(src)

def _segment_sum(src, seg, n):
    return jax.ops.segment_sum(src, seg, n)
kernel_name = 'mk_adj_preln_d1_adj_r2_6c22e1'

def setup_inputs(seed: int=0):
    np.random.seed(seed)
    _w = jnp.asarray

    def _rec_inputs():
        import jax
        import jax.numpy as jnp
        _gk = jax.random.key(seed)
        x = -0.000929 + 1 * jax.random.normal(jax.random.fold_in(_gk, 1), (4096, 128), jnp.float32)
        _a = jax.random.bernoulli(jax.random.fold_in(_gk, 2), 0.000488281, (4096, 4096))
        _a = jnp.logical_or(_a, jnp.swapaxes(_a, -1, -2))
        _a = jnp.logical_or(_a, jnp.eye(4096, dtype=bool))
        _af = _a.astype(jnp.float32)
        _af = _af * jax.random.uniform(jax.random.fold_in(_gk, 3), (4096, 4096), jnp.float32, 0.05, 1)
        adj = _af
        return (x, adj)
    x, adj = _rec_inputs()

    def _L0_gnn_setup():
        import jax, jax.numpy as jnp
        import numpy as np
        NEG_SLOPE = 0.01
        N_U, N_V = (4096, 4096)
        U_F, V_F = (128, 128)
        HIDS = [128, 128]
        NUM_ROUNDS = 3

        def _glorot(key, fan_in, fan_out):
            lim = np.sqrt(6.0 / (fan_in + fan_out)).astype(np.float32)
            return jax.random.uniform(key, (fan_in, fan_out), jnp.float32, -lim, lim)

        def _mlp(x, W1, b1, W2, b2, W3, b3):
            a = jax.nn.leaky_relu
            x = a(x @ W1 + b1, NEG_SLOPE)
            x = a(x @ W2 + b2, NEG_SLOPE)
            return a(x @ W3 + b3, NEG_SLOPE)
        key = jax.random.key(seed)
        ks = jax.random.split(key, 12)
        inp = {'u_node_feats': jax.random.normal(ks[0], (N_U, U_F), jnp.float32), 'v_node_feats': jax.random.normal(ks[1], (N_V, V_F), jnp.float32), 'uv_adj_mat': jax.random.uniform(ks[2], (N_V, N_U), jnp.float32), 'vu_adj_mat': jax.random.uniform(ks[3], (N_U, N_V), jnp.float32)}
        dims_uv = [U_F] + HIDS + [V_F]
        dims_vu = [V_F] + HIDS + [U_F]
        k = 4
        for tag, dims in (('uv', dims_uv), ('vu', dims_vu)):
            for i in range(3):
                inp[f'{tag}_W{i + 1}'] = _glorot(ks[k], dims[i], dims[i + 1])
                k += 1
                inp[f'{tag}_b{i + 1}'] = jnp.zeros((dims[i + 1],), jnp.float32)
        return inp
    _L0_gnn_all = _L0_gnn_setup()
    _L0_gnn_in = {k: v for k, v in _L0_gnn_all.items() if k in ('v_node_feats', 'uv_W1', 'uv_b1', 'uv_W2', 'uv_b2', 'uv_W3', 'uv_b3', 'vu_W1', 'vu_b1', 'vu_W2', 'vu_b2', 'vu_W3', 'vu_b3')}
    del _L0_gnn_all
    return {'x': x, 'adj': adj, 'L0_gnn_v_node_feats': _L0_gnn_in['v_node_feats'], 'L0_gnn_uv_W1': _L0_gnn_in['uv_W1'], 'L0_gnn_uv_b1': _L0_gnn_in['uv_b1'], 'L0_gnn_uv_W2': _L0_gnn_in['uv_W2'], 'L0_gnn_uv_b2': _L0_gnn_in['uv_b2'], 'L0_gnn_uv_W3': _L0_gnn_in['uv_W3'], 'L0_gnn_uv_b3': _L0_gnn_in['uv_b3'], 'L0_gnn_vu_W1': _L0_gnn_in['vu_W1'], 'L0_gnn_vu_b1': _L0_gnn_in['vu_b1'], 'L0_gnn_vu_W2': _L0_gnn_in['vu_W2'], 'L0_gnn_vu_b2': _L0_gnn_in['vu_b2'], 'L0_gnn_vu_W3': _L0_gnn_in['vu_W3'], 'L0_gnn_vu_b3': _L0_gnn_in['vu_b3']}

def reference(x, adj, L0_gnn_v_node_feats, L0_gnn_uv_W1, L0_gnn_uv_b1, L0_gnn_uv_W2, L0_gnn_uv_b2, L0_gnn_uv_W3, L0_gnn_uv_b3, L0_gnn_vu_W1, L0_gnn_vu_b1, L0_gnn_vu_W2, L0_gnn_vu_b2, L0_gnn_vu_W3, L0_gnn_vu_b3):
    import jax
    import jax.numpy as jnp

    def _L0_gnn_ref(u_node_feats, v_node_feats, uv_adj_mat, vu_adj_mat, uv_W1, uv_b1, uv_W2, uv_b2, uv_W3, uv_b3, vu_W1, vu_b1, vu_W2, vu_b2, vu_W3, vu_b3):
        import jax, jax.numpy as jnp
        import numpy as np
        NEG_SLOPE = 0.01
        N_U, N_V = (4096, 4096)
        U_F, V_F = (128, 128)
        HIDS = [128, 128]
        NUM_ROUNDS = 3

        def _glorot(key, fan_in, fan_out):
            lim = np.sqrt(6.0 / (fan_in + fan_out)).astype(np.float32)
            return jax.random.uniform(key, (fan_in, fan_out), jnp.float32, -lim, lim)

        def _mlp(x, W1, b1, W2, b2, W3, b3):
            a = jax.nn.leaky_relu
            x = a(x @ W1 + b1, NEG_SLOPE)
            x = a(x @ W2 + b2, NEG_SLOPE)
            return a(x @ W3 + b3, NEG_SLOPE)
        u, v = (u_node_feats, v_node_feats)
        for _ in range(NUM_ROUNDS):
            v = _mlp(uv_adj_mat @ u, uv_W1, uv_b1, uv_W2, uv_b2, uv_W3, uv_b3)
            u = _mlp(vu_adj_mat @ v, vu_W1, vu_b1, vu_W2, vu_b2, vu_W3, vu_b3)
        return v
    h = jnp.maximum(_layernorm(x, axis=-1), 0.0)
    x = x + _L0_gnn_ref(h, L0_gnn_v_node_feats, adj, adj, L0_gnn_uv_W1, L0_gnn_uv_b1, L0_gnn_uv_W2, L0_gnn_uv_b2, L0_gnn_uv_W3, L0_gnn_uv_b3, L0_gnn_vu_W1, L0_gnn_vu_b1, L0_gnn_vu_W2, L0_gnn_vu_b2, L0_gnn_vu_W3, L0_gnn_vu_b3)
    return x

_drawn_inputs = setup_inputs


def setup_inputs(seed=0):
    import zlib

    import numpy as np

    out = dict(_drawn_inputs(seed))
    spreads = {'L0_gnn_uv_b1': (0.0, 0.294),
     'L0_gnn_uv_b2': (0.0, 0.1),
     'L0_gnn_uv_b3': (0.0, 0.1),
     'L0_gnn_vu_b1': (0.0, 0.1),
     'L0_gnn_vu_b2': (0.0, 0.1),
     'L0_gnn_vu_b3': (0.0, 0.1)}
    factors = {}
    for name, (base, spread) in spreads.items():
        noise = np.random.default_rng([zlib.crc32(name.encode()), seed]).standard_normal(out[name].shape)
        drawn = base * np.exp(spread * noise) if base else spread * noise
        out[name] = jnp.asarray(drawn.astype(out[name].dtype))
    for name, factor in factors.items():
        out[name] = (out[name] * factor).astype(out[name].dtype)
    return out
```

```python
import concourse.bass as bass
from concourse import mybir
from contextlib import ExitStack

F32 = mybir.dt.float32
F32R = mybir.dt.float32r
ALU = mybir.AluOpType
ACT = mybir.ActivationFunctionType

P = 128
KT = 4
B = KT * P
RAW = 4
SPLIT = 5
LAG = 2
SLOPE = 0.01
EPS = 1e-5
LAST = 5


def sweep_blocks(NB):
    blocks = []
    for i in range(NB):
        upper = [(i, j, 1, None) for j in range(i + 1, NB)]
        lower = [(i, j, 1, 2) for j in range(i)]
        while upper or lower:
            if upper:
                blocks.append(upper.pop(0))
            if lower and (len(lower) > 1 or not upper):
                blocks.append(lower.pop(0))
        blocks.append((i, i, 1, 2))
    for p in (2, 4):
        for i in range(NB - 2, -1, -1):
            blocks += [(i, j, p, p + 1) for j in range(NB - 1, i, -1)]
        for i in range(NB):
            blocks += [(i, j, p + 1, p + 2 if p + 2 <= LAST else None) for j in range(i + 1)]
    return blocks


def plan(blocks, NB):
    PRODUCT, LAYER, EVACUATE, SPLIT_Y = 2.6, 0.9, 2.0, 4.0
    want = {}
    for i, j, p, q in blocks:
        want[(p, i)] = want.get((p, i), 0) + 1
        if q:
            want[(q, i)] = want.get((q, i), 0) + 1
    total = dict(want)
    left_in_row = {}
    rows = []
    for t, (i, j, p, q) in enumerate(blocks):
        if not rows or rows[-1][:2] != (p, i):
            rows.append((p, i, []))
        rows[-1][2].append(t)
    known = {(0, j): 0.0 for j in range(NB)}
    order, jobs, waiting = [], [], []
    lead = trail = 0
    trails = [t for t, blk in enumerate(blocks) if blk[3]]
    freed = {}
    now = 0.0

    def product(kind, t):
        nonlocal now
        i, j, p, q = blocks[t]
        r = p if kind == "lead" else q
        now += PRODUCT
        order.append((kind, t))
        want[(r, i)] -= 1
        if want[(r, i)] == 0:
            jobs.append((r, i, kind, t))
            waiting.append([now + EVACUATE, 1, len(jobs) - 1])

    while lead < len(blocks) or trail < len(trails) or waiting:
        due = [w for w in waiting if w[0] <= now]
        if due:
            w = min(due, key=lambda w: (w[2], w[1]))
            waiting.remove(w)
            now += LAYER
            order.append((f"layer{w[1]}", w[2]))
            if w[1] < 3:
                waiting.append([now + EVACUATE, w[1] + 1, w[2]])
            else:
                known[jobs[w[2]][:2]] = now + SPLIT_Y
            continue
        can_lead = lead < len(blocks) and known.get((blocks[lead][2] - 1, blocks[lead][1]), 1e9) <= now
        at = trails[trail] if trail < len(trails) else None
        can_trail = at is not None and at < lead and known.get((blocks[at][3] - 1, blocks[at][1]), 1e9) <= now
        room = at is None or lead - at < SPLIT - 1
        if can_trail and (lead - at > LAG or not can_lead or not room):
            product("trail", at)
            trail += 1
        elif can_lead and room:
            product("lead", lead)
            lead += 1
        else:
            now += 0.1
    return order, jobs, total


def build(nc, x, adj_blocks, weights, biases, out):
    NB = adj_blocks.shape[0]
    N = NB * B
    blocks = sweep_blocks(NB)
    order, jobs, total = plan(blocks, NB)
    job_of = {(p, i): m for m, (p, i, _, _) in enumerate(jobs)}

    product_no, last_use = {}, {}
    for kind, t in order:
        if kind in ("lead", "trail"):
            product_no[(kind, t)] = len(product_no)
            last_use[t] = product_no[(kind, t)]
    group = {"lead": {}, "trail": {}}
    first, last, groups = set(), {}, {"lead": [], "trail": []}
    for kind, slot in (("lead", 2), ("trail", 3)):
        previous = None
        for t, blk in enumerate(blocks):
            if not blk[slot]:
                continue
            key = (blk[slot], blk[0])
            if key != previous:
                first.add((kind, t))
                groups[kind].append(key)
                previous = key
            group[kind][t] = len(groups[kind]) - 1
            last[(kind, len(groups[kind]) - 1)] = t
    row_end = {(kind, t): g for (kind, g), t in last.items()}
    job_end = {(kind, t): m for m, (_, _, kind, t) in enumerate(jobs)}
    saves = [(e, blocks[e[1]][3], blocks[e[1]][0]) for e in order if e in row_end and e not in job_end]
    assert all(e[0] == "trail" for e, _, _ in saves)
    save_no = {e: n for n, (e, _, _) in enumerate(saves)}
    saved_as = {(p, i): n for n, (_, p, i) in enumerate(saves)}
    enables, latest = {}, 0
    for t in range(SPLIT, len(blocks)):
        latest = max(latest, last_use[t - SPLIT])
        enables.setdefault(latest, []).append(t)

    with ExitStack() as ctx:
        def sbuf(name, shape, dt=F32):
            return ctx.enter_context(nc.sbuf_tensor(name, shape, dt))

        def psum(name):
            return ctx.enter_context(nc.psum_tensor(name, [P, B], F32))

        def sem(name):
            return ctx.enter_context(nc.semaphore(name))

        raw = [sbuf(f"raw{k}", [P, KT * B]) for k in range(RAW)]
        a_hi = [sbuf(f"a_hi{k}", [P, KT * B], F32R) for k in range(SPLIT)]
        a_lo = [sbuf(f"a_lo{k}", [P, KT * B], F32R) for k in range(SPLIT)]
        y_hi = [sbuf(f"y_hi{g}", [P, N], F32R) for g in range(2)]
        y_lo = [sbuf(f"y_lo{g}", [P, N], F32R) for g in range(2)]
        partial = [sbuf(f"partial{i}", [P, B]) for i in range(NB)]
        x0 = sbuf("x0", [P, B])
        h1 = sbuf("h1", [P, B])
        h2 = sbuf("h2", [P, B])
        yv = sbuf("yv", [P, B])
        w_sb = [[sbuf(f"w{s}{n}", [P, P]) for n in range(3)] for s in range(2)]
        b_sb = [[sbuf(f"b{s}{n}", [P, 1]) for n in range(2)] for s in range(2)]
        b3_sb = [sbuf(f"b3_{s}", [P, P]) for s in range(2)]
        stats = sbuf("stats", [P, KT, 6])
        moments = sbuf("moments", [P, KT, 2])
        std = sbuf("std", [P, KT])
        rstd = sbuf("rstd", [P, KT])

        bank = {"lead": [psum(f"lead{k}") for k in range(2)],
                "trail": [psum(f"trail{k}") for k in range(2)]}
        ps1, ps2, ps3 = psum("ps1"), psum("ps2"), psum("ps3")

        weights_landed = sem("weights_landed")
        x_landed = [sem(f"x_landed{j}") for j in range(NB)]
        raw_landed = [sem(f"raw_landed{k}") for k in range(RAW)]
        hi_ready = sem("hi_ready")
        lo_ready = sem("lo_ready")
        products = sem("products")
        saved = sem("saved")
        x0_ready = sem("x0_ready")
        layer_done = [sem(f"layer{n + 1}_done") for n in range(3)]
        bias1_done = sem("bias1_done")
        bias2_done = sem("bias2_done")
        h1_ready = sem("h1_ready")
        h2_ready = sem("h2_ready")
        bias3_done = sem("bias3_done")
        relu3_done = sem("relu3_done")
        y_hi_ready = sem("y_hi_ready")
        y_ready = sem("y_ready")
        norm_step = sem("norm_step")
        var_ready = sem("var_ready")
        std_ready = sem("std_ready")
        centred = sem("centred")
        relu_ready = sem("relu_ready")
        h_ready = sem("h_ready")
        x_again = [sem(f"x_again{i}") for i in range(NB)]
        out_written = sem("out_written")

        block = ctx.enter_context(nc.Block())
        h_order = [blocks[n][1] for n in range(NB)]

        def x_rows(i):
            return x[i * B:(i + 1) * B, :].rearrange("(k p) f -> p k f", p=P)

        def tiles(buf):
            return buf[:, :].rearrange("p (k f) -> p k f", f=P)

        def final(m):
            return jobs[m][0] == LAST

        def y_at(m):
            p, i = jobs[m][:2]
            return (y_hi[p % 2][:, i * B:(i + 1) * B], y_lo[p % 2][:, i * B:(i + 1) * B])

        def splits_before(m):
            return sum(not final(k) for k in range(m))

        @block.sync
        def _(sp):
            for t, (i, j, _, _) in enumerate(blocks):
                if t < NB:
                    sp.dma_start(tiles(partial[h_order[t]]), x_rows(h_order[t])).then_inc(x_landed[h_order[t]], 16)
                if t >= RAW:
                    sp.wait_ge(lo_ready, t - RAW + 1)
                sp.dma_start(raw[t % RAW][:, :], adj_blocks[i, j, :, :]).then_inc(raw_landed[t % RAW], 16)

        @block.gpsimd
        def _(pool):
            ends = [m for m in range(len(jobs)) if final(m)]

            def store(m):
                i = jobs[m][1]
                pool.wait_ge(y_ready, m + 1)
                pool.dma_start(out[i * B:(i + 1) * B, :].rearrange("(k p) f -> p k f", p=P),
                               tiles(partial[i])).then_inc(out_written, 16)

            for n, m in enumerate(ends):
                i = jobs[m][1]
                pool.wait_ge(x0_ready, m + 1)
                pool.dma_start(tiles(partial[i]), x_rows(i)).then_inc(x_again[i], 16)
                if n:
                    store(ends[n - 1])
            store(ends[-1])
            pool.wait_ge(out_written, 16 * len(ends))

        @block.scalar
        def _(act):
            for s in range(2):
                for n in range(3):
                    act.dma_start(w_sb[s][n][:, :], weights[s][n]).then_inc(weights_landed, 16)
                for n in range(2):
                    act.dma_start(b_sb[s][n][:, :], biases[s][n].rearrange("(p a) -> p a", a=1))\
                        .then_inc(weights_landed, 16)
                act.dma_start(b3_sb[s][:, :], biases[s][2].partition_broadcast(P))\
                    .then_inc(weights_landed, 16)

            def split_hi(t):
                if t >= SPLIT:
                    act.wait_ge(products, last_use[t - SPLIT] + 1)
                act.wait_ge(raw_landed[t % RAW], 16 * (t // RAW + 1))
                act.activation(a_hi[t % SPLIT][:, :], raw[t % RAW][:, :], ACT.Copy).then_inc(hi_ready, 1)

            for n, j in enumerate(h_order):
                act.wait_ge(var_ready, n + 1)
                act.activation(std[:, :], std[:, :], ACT.Sqrt).then_inc(std_ready, 1)
                act.wait_ge(centred, n + 1)
                act.activation(y_hi[0][:, j * B:(j + 1) * B], yv[:, :], ACT.Relu).then_inc(relu_ready, 1)
                if n < SPLIT:
                    split_hi(n)

            act.wait_ge(weights_landed, 16 * 12)
            for kind, a in order:
                if kind in ("lead", "trail"):
                    for t in enables.get(product_no[(kind, a)], []):
                        split_hi(t)
                    continue
                m, s = a, 1 - jobs[a][0] % 2
                if kind == "layer1":
                    act.wait_ge(layer_done[0], m + 1)
                    if m >= 1:
                        act.wait_ge(layer_done[1], m)
                    act.activation(h1[:, :], ps1[:, :], ACT.Identity, bias=b_sb[s][0][:, 0:1]).then_inc(bias1_done, 1)
                elif kind == "layer2":
                    act.wait_ge(layer_done[1], m + 1)
                    if m >= 1:
                        act.wait_ge(layer_done[2], m)
                    act.activation(h2[:, :], ps2[:, :], ACT.Identity, bias=b_sb[s][1][:, 0:1]).then_inc(bias2_done, 1)
                elif not final(m):
                    act.wait_ge(relu3_done, m + 1)
                    act.activation(y_at(m)[0], yv[:, :], ACT.Copy).then_inc(y_hi_ready, 1)

        @block.vector
        def _(dve):
            step = [0]

            def own(ins):
                step[0] += 1
                ins.then_inc(norm_step, 1)
                dve.wait_ge(norm_step, step[0])

            def leaky_relu(h):
                return dve.scalar_tensor_tensor(out=h[:, :], in0=h[:, :], scalar=SLOPE, in1=h[:, :],
                                                op0=ALU.mult, op1=ALU.max)

            def split_lo(t):
                dve.wait_ge(hi_ready, t + 1)
                k = t % SPLIT
                dve.tensor_tensor(a_lo[k][:, :], raw[t % RAW][:, :], a_hi[k][:, :].bitcast(F32),
                                  ALU.subtract).then_inc(lo_ready, 1)

            for n, j in enumerate(h_order):
                dve.wait_ge(x_landed[j], 16)
                for k in range(KT):
                    ins = dve.bn_stats(stats[:, k, :], partial[j][:, k * P:(k + 1) * P])
                own(ins)
                for k in range(KT):
                    ins = dve.bn_aggr(moments[:, k, :], stats[:, k, :])
                own(ins)
                dve.tensor_scalar(std[:, :], moments[:, :, 1], EPS, None, ALU.add).then_inc(var_ready, 1)
                dve.wait_ge(std_ready, n + 1)
                own(dve.reciprocal(rstd[:, :], std[:, :]))
                if n:
                    dve.wait_ge(h_ready, n)
                for k in range(KT):
                    ins = dve.tensor_scalar(yv[:, k * P:(k + 1) * P], partial[j][:, k * P:(k + 1) * P],
                                            moments[:, k, 0:1], rstd[:, k:k + 1], ALU.subtract, ALU.mult)
                ins.then_inc(centred, 1)
                dve.wait_ge(relu_ready, n + 1)
                at = slice(j * B, (j + 1) * B)
                dve.scalar_tensor_tensor(out=y_lo[0][:, at], in0=yv[:, :], scalar=0.0,
                                         in1=y_hi[0][:, at].bitcast(F32), op0=ALU.max, op1=ALU.subtract)\
                    .then_inc(h_ready, 1)
                if n < SPLIT:
                    split_lo(n)

            dve.wait_ge(weights_landed, 16 * 12)
            for kind, a in order:
                if kind in ("lead", "trail"):
                    t, e = a, (kind, a)
                    src = bank[kind][group[kind][t] % 2]
                    if e in job_end:
                        m = job_end[e]
                        p, i = jobs[m][:2]
                        dve.wait_ge(products, product_no[e] + 1)
                        if m >= 1:
                            dve.wait_ge(layer_done[0], m)
                        if (p, i) in saved_as:
                            dve.wait_ge(saved, saved_as[(p, i)] + 1)
                            ins = dve.tensor_tensor(x0[:, :], src[:, :], partial[i][:, :], ALU.add)
                        else:
                            ins = dve.tensor_copy(x0[:, :], src[:, :])
                        ins.then_inc(x0_ready, 1)
                    elif e in save_no:
                        i = blocks[t][0]
                        dve.wait_ge(products, product_no[e] + 1)
                        dve.tensor_copy(partial[i][:, :], src[:, :]).then_inc(saved, 1)
                    for t in enables.get(product_no[e], []):
                        split_lo(t)
                elif kind in ("layer1", "layer2"):
                    m = a
                    h, biased, ready = (h1, bias1_done, h1_ready) if kind == "layer1" else (h2, bias2_done, h2_ready)
                    dve.wait_ge(biased, m + 1)
                    leaky_relu(h).then_inc(ready, 1)
                elif kind == "layer3":
                    m = a
                    p, i = jobs[m][:2]
                    dve.wait_ge(layer_done[2], m + 1)
                    if m >= 1:
                        dve.wait_ge(y_ready, m)
                    dve.tensor_tensor(tiles(yv), tiles(ps3),
                                      b3_sb[1 - p % 2][:, :].unsqueeze(1).to_broadcast([P, KT, P]),
                                      ALU.add).then_inc(bias3_done, 1)
                    dve.wait_ge(bias3_done, m + 1)
                    leaky_relu(yv).then_inc(relu3_done, 1)
                    if final(m):
                        dve.wait_ge(relu3_done, m + 1)
                        dve.wait_ge(x_again[i], 16)
                        dve.tensor_tensor(partial[i][:, :], partial[i][:, :], yv[:, :], ALU.add)\
                            .then_inc(y_ready, 1)
                    else:
                        hi, lo = y_at(m)
                        dve.wait_ge(y_hi_ready, splits_before(m) + 1)
                        dve.tensor_tensor(lo, yv[:, :], hi.bitcast(F32), ALU.subtract).then_inc(y_ready, 1)

        @block.tensor
        def _(pe):
            pe.wait_ge(weights_landed, 16 * 12)
            for kind, a in order:
                if kind in ("lead", "trail"):
                    t, e = a, (kind, a)
                    i, j, p, q = blocks[t]
                    r = p if kind == "lead" else q
                    g = group[kind][t]
                    dst = bank[kind][g % 2][:, :]
                    pe.wait_ge(lo_ready, t + 1)
                    if r == 1:
                        pe.wait_ge(h_ready, h_order.index(j) + 1)
                    else:
                        pe.wait_ge(y_ready, job_of[(r - 1, j)] + 1)
                    if e in first and g >= 2:
                        before = (kind, last[(kind, g - 2)])
                        if before in job_end:
                            pe.wait_ge(x0_ready, job_end[before] + 1)
                        else:
                            pe.wait_ge(saved, save_no[before] + 1)
                    for k in range(KT):
                        yk = slice((j * KT + k) * P, (j * KT + k + 1) * P)
                        ak = slice(k * B, (k + 1) * B)
                        yh, yl = y_hi[(r - 1) % 2][:, yk], y_lo[(r - 1) % 2][:, yk]
                        ah, al = a_hi[t % SPLIT][:, ak], a_lo[t % SPLIT][:, ak]
                        pe.matmul(dst, yh, ah, start=(e in first and k == 0), stop=False)
                        pe.matmul(dst, yh, al, start=False, stop=False)
                        ins = pe.matmul(dst, yl, ah, start=False, stop=(e in row_end and k == KT - 1))
                    ins.then_inc(products, 1)
                    continue
                m, s = a, 1 - jobs[a][0] % 2
                w = w_sb[s][int(kind[-1]) - 1][:, :]
                if kind == "layer1":
                    pe.wait_ge(x0_ready, m + 1)
                    if m >= 1:
                        pe.wait_ge(h1_ready, m)
                    pe.matmul(ps1[:, :], w, x0[:, :], start=True, stop=True).then_inc(layer_done[0], 1)
                elif kind == "layer2":
                    pe.wait_ge(h1_ready, m + 1)
                    if m >= 1:
                        pe.wait_ge(h2_ready, m)
                    pe.matmul(ps2[:, :], w, h1[:, :], start=True, stop=True).then_inc(layer_done[1], 1)
                else:
                    pe.wait_ge(h2_ready, m + 1)
                    if m >= 1:
                        pe.wait_ge(bias3_done, m)
                    for k in range(KT):
                        ins = pe.matmul(ps3[:, k * P:(k + 1) * P], h2[:, k * P:(k + 1) * P], w,
                                        start=True, stop=True)
                    ins.then_inc(layer_done[2], 1)


def kernel(x, adj, L0_gnn_v_node_feats, L0_gnn_uv_W1, L0_gnn_uv_b1, L0_gnn_uv_W2, L0_gnn_uv_b2,
           L0_gnn_uv_W3, L0_gnn_uv_b3, L0_gnn_vu_W1, L0_gnn_vu_b1, L0_gnn_vu_W2, L0_gnn_vu_b2,
           L0_gnn_vu_W3, L0_gnn_vu_b3):
    import numpy as np
    import concourse.bacc as bacc
    from concourse.bass_utils import run_bass_kernel_spmd

    x = np.asarray(x)
    nb = x.shape[0] // B
    blocks = np.ascontiguousarray(np.asarray(adj).reshape(nb, B, nb, KT, P).transpose(0, 2, 4, 3, 1)
                                  .reshape(nb, nb, P, KT * B))
    arrays = {"x": x, "adj_blocks": blocks}
    for side, ws in (("uv", (L0_gnn_uv_W1, L0_gnn_uv_W2, L0_gnn_uv_W3)),
                     ("vu", (L0_gnn_vu_W1, L0_gnn_vu_W2, L0_gnn_vu_W3))):
        for n, w in enumerate(ws):
            arrays[f"{side}_w{n + 1}"] = np.asarray(w)
    for side, bs in (("uv", (L0_gnn_uv_b1, L0_gnn_uv_b2, L0_gnn_uv_b3)),
                     ("vu", (L0_gnn_vu_b1, L0_gnn_vu_b2, L0_gnn_vu_b3))):
        for n, b in enumerate(bs):
            arrays[f"{side}_b{n + 1}"] = np.asarray(b)
    nc = bacc.Bacc("TRN2", target_bir_lowering=False, num_devices=1)
    ap = {name: nc.dram_tensor(name, a.shape, mybir.dt.from_np(a.dtype), kind="ExternalInput").ap()
          for name, a in arrays.items()}
    out = nc.dram_tensor("out", x.shape, mybir.dt.from_np(x.dtype), kind="ExternalOutput").ap()
    build(nc, ap["x"], ap["adj_blocks"],
          [[ap[f"{side}_w{n + 1}"] for n in range(3)] for side in ("uv", "vu")],
          [[ap[f"{side}_b{n + 1}"] for n in range(3)] for side in ("uv", "vu")], out)
    return run_bass_kernel_spmd(nc, [arrays], core_ids=[0]).results[0]["out"]
```

```python
import concourse.bass as bass
from concourse import mybir
from contextlib import ExitStack

F32 = mybir.dt.float32
F32R = mybir.dt.float32r
ALU = mybir.AluOpType
ACT = mybir.ActivationFunctionType

P = 128
KT = 4
B = KT * P
RAW = 4
SPLIT = 5
LAG = 2
AHEAD = 2
TUNE = (1.3, 3.0, 5.0)
SLOPE = 0.01
EPS = 1e-5
LAST = 5


def sweep_blocks(NB):
    def first_sweep(i):
        upper = [(i, j, 1, None) for j in range(i + 1, NB)]
        lower = [(i, j, 1, 2) for j in range(i)]
        row = []
        while upper or lower:
            if upper:
                row.append(upper.pop(0))
            if lower and (len(lower) > 1 or not upper):
                row.append(lower.pop(0))
        return row + [(i, i, 1, 2)]

    blocks = [(i, j, 1, None) for j in range(2, NB) for i in (0, 1)]
    blocks += [(0, 1, 1, None), (1, 1, 1, 2), (0, 0, 1, 2), (1, 0, 1, 2)]
    for i in range(2, NB):
        blocks += first_sweep(i)
    for p in (2, 4):
        up = [(i, j, p, p + 1) for i in range(NB - 2, -1, -1) for j in range(NB - 1, i, -1)]
        down = [(i, j, p + 1, p + 2 if p + 2 <= LAST else None) for i in range(NB) for j in range(i + 1)]
        up.insert(0, up.pop(2))
        down.insert(0, down.pop(2))
        blocks += up + down
    return blocks


def plan(blocks, NB):
    PRODUCT, LAYER, TO_LAYER1, TO_NEXT, TO_Y = 2.6, 0.9, TUNE[0], TUNE[1], TUNE[2]
    LOAD, SPLIT_TIME = 2.8, 2.6
    need, rows, seen = {}, {}, {}
    for t, (i, j, p, q) in enumerate(blocks):
        for kind, r in (("lead", p), ("trail", q)):
            if r:
                need[(r, i)] = need.get((r, i), 0) + 1
                rows[(kind, r, i)] = rows.get((kind, r, i), 0) + 1
    known = {(0, j): 4.0 + 4.0 * ((j - 2) % NB) for j in range(NB)}
    order, jobs, waiting, splits = [], [], [], {}
    slot, ready, loaded = {}, {}, []
    groups, open_groups = {}, {"lead": [], "trail": []}
    bank_free = {"lead": [(0, None), (1, None)], "trail": [(0, None), (1, None)]}
    todo = {("lead", t) for t in range(len(blocks))} | {("trail", t) for t in range(len(blocks)) if blocks[t][3]}
    done = set()
    layer_done = [0, 0, 0]
    now = 0.0

    def take_slot(k, at):
        t = len(slot)
        if t == len(blocks):
            return
        start = max(loaded[-1] if loaded else 2.0, ready[t - RAW] + 2.0 if t >= RAW else 0.0)
        loaded.append(start + LOAD)
        ready[t] = max(loaded[-1], at, ready[t - 1] if t else 0.0) + SPLIT_TIME
        slot[t] = k
        splits.setdefault(len(order) - 1, []).append(t)

    def key_of(kind, t):
        i, _, p, q = blocks[t]
        return (kind, p if kind == "lead" else q, i)

    def when(kind, t):
        key = key_of(kind, t)
        y = (key[1] - 1, blocks[t][1])
        if t not in slot or y not in known or (kind == "trail" and ("lead", t) not in done):
            return None
        if key not in groups and not bank_free[kind]:
            return None
        if need[key[1:]] == 1 and len(jobs) > layer_done[0]:
            return None
        return max(known[y], ready[t])

    def product(kind, t):
        nonlocal now
        key = key_of(kind, t)
        if key not in groups:
            groups[key] = bank_free[kind].pop(0)
        todo.discard((kind, t))
        done.add((kind, t))
        order.append((kind, t))
        now += PRODUCT
        rows[key] -= 1
        need[key[1:]] -= 1
        if rows[key] == 0:
            bank_free[kind].append((groups[key][0], key))
            if need[key[1:]] == 0:
                jobs.append((key[1], key[2], kind, t))
                waiting.append([now + TO_LAYER1, 1, len(jobs) - 1])
        if kind == "trail" or not blocks[t][3]:
            take_slot(slot[t], now)

    for k in range(SPLIT):
        take_slot(k, 0.0)
    while todo or waiting:
        able = [w for w in waiting if w[1] == 3 or layer_done[w[1]] >= w[2]]
        able = [w for w in able if layer_done[w[1] - 1] == w[2]]
        due = [w for w in able if w[0] <= now]
        if due:
            w = min(due, key=lambda w: w[2])
            waiting.remove(w)
            now += LAYER
            order.append((f"layer{w[1]}", w[2]))
            layer_done[w[1] - 1] += 1
            if w[1] < 3:
                waiting.append([now + TO_NEXT, w[1] + 1, w[2]])
            else:
                known[jobs[w[2]][:2]] = now + TO_Y
            continue
        leads = [("lead", t) for t in range(len(blocks)) if ("lead", t) in todo and t in slot]
        trails = [("trail", t) for t in range(len(blocks)) if ("trail", t) in todo and ("lead", t) in done]
        times = {e: when(*e) for e in leads + trails}
        go_lead = [e for e in leads if times[e] is not None and times[e] <= now]
        go_trail = [e for e in trails if times[e] is not None and times[e] <= now]
        if go_trail and (not go_lead or len(trails) > LAG):
            product(*go_trail[0])
        elif go_lead:
            product(*go_lead[0])
        else:
            later = [t for t in list(times.values()) + [w[0] for w in able] if t is not None]
            now = max(now + 0.05, min(later))
    plan.time = now
    return order, jobs, splits, slot, groups


def build(nc, x, adj_blocks, weights, biases, out):
    NB = adj_blocks.shape[0]
    N = NB * B
    blocks = sweep_blocks(NB)
    order, jobs, splits, slot, groups = plan(blocks, NB)
    job_of = {(p, i): m for m, (p, i, _, _) in enumerate(jobs)}

    product_no, last_use = {}, {}
    for kind, a in order:
        if kind in ("lead", "trail"):
            product_no[(kind, a)] = len(product_no) + 1
            last_use[a] = product_no[(kind, a)]
    before_in_slot, holder = {}, {}
    for t in range(len(blocks)):
        before_in_slot[t] = holder.get(slot[t])
        holder[slot[t]] = t

    def row_of(kind, t):
        return (kind, blocks[t][2 if kind == "lead" else 3], blocks[t][0])

    first, last = {}, {}
    for e in product_no:
        first.setdefault(row_of(*e), e)
        last[row_of(*e)] = e
    job_end = {(kind, t): m for m, (_, _, kind, t) in enumerate(jobs)}
    saves = [e for e in product_no if last[row_of(*e)] == e and e not in job_end]
    assert all(kind == "trail" for kind, _ in saves)
    save_no = {e: n + 1 for n, e in enumerate(saves)}
    saved_as = {row_of(*e)[1:]: n for e, n in save_no.items()}

    with ExitStack() as ctx:
        def sbuf(name, shape, dt=F32):
            return ctx.enter_context(nc.sbuf_tensor(name, shape, dt))

        def psum(name):
            return ctx.enter_context(nc.psum_tensor(name, [P, B], F32))

        def sem(name):
            return ctx.enter_context(nc.semaphore(name))

        raw = [sbuf(f"raw{k}", [P, KT * B]) for k in range(RAW)]
        a_hi = [sbuf(f"a_hi{k}", [P, KT * B], F32R) for k in range(SPLIT)]
        a_lo = [sbuf(f"a_lo{k}", [P, KT * B], F32R) for k in range(SPLIT)]
        y_hi = [sbuf(f"y_hi{g}", [P, N], F32R) for g in range(2)]
        y_lo = [sbuf(f"y_lo{g}", [P, N], F32R) for g in range(2)]
        partial = [sbuf(f"partial{i}", [P, B]) for i in range(NB)]
        x0 = sbuf("x0", [P, B])
        h1 = sbuf("h1", [P, B])
        h2 = sbuf("h2", [P, B])
        yv = sbuf("yv", [P, B])
        w_sb = [[sbuf(f"w{s}{n}", [P, P]) for n in range(3)] for s in range(2)]
        b_sb = [[sbuf(f"b{s}{n}", [P, 1]) for n in range(2)] for s in range(2)]
        b3_sb = [sbuf(f"b3_{s}", [P, P]) for s in range(2)]
        stats = sbuf("stats", [P, KT, 6])
        moments = sbuf("moments", [P, NB * KT, 2])
        std = sbuf("std", [P, NB * KT])
        rstd = sbuf("rstd", [P, NB * KT])
        shift = sbuf("shift", [P, NB * KT])

        bank = {"lead": [psum(f"lead{k}") for k in range(2)],
                "trail": [psum(f"trail{k}") for k in range(2)]}
        ps1, ps2, ps3 = psum("ps1"), psum("ps2"), psum("ps3")

        weights_landed = sem("weights_landed")
        x_landed = [sem(f"x_landed{j}") for j in range(NB)]
        raw_landed = [sem(f"raw_landed{k}") for k in range(RAW)]
        hi_ready = sem("hi_ready")
        lo_ready = sem("lo_ready")
        products = sem("products")
        saved = sem("saved")
        x0_ready = sem("x0_ready")
        layer_done = [sem(f"layer{n + 1}_done") for n in range(3)]
        bias1_done = sem("bias1_done")
        bias2_done = sem("bias2_done")
        h1_ready = sem("h1_ready")
        h2_ready = sem("h2_ready")
        bias3_done = sem("bias3_done")
        relu3_done = sem("relu3_done")
        y_hi_ready = sem("y_hi_ready")
        y_ready = sem("y_ready")
        norm_step = sem("norm_step")
        var_ready = sem("var_ready")
        std_ready = sem("std_ready")
        rstd_ready = sem("rstd_ready")
        scaled = sem("scaled")
        relu_ready = sem("relu_ready")
        y0_hi_ready = sem("y0_hi_ready")
        h_ready = sem("h_ready")
        x_again = [sem(f"x_again{i}") for i in range(NB)]
        out_written = sem("out_written")

        block = ctx.enter_context(nc.Block())
        h_order = []
        for _, j, _, _ in blocks:
            if j not in h_order:
                h_order.append(j)
        assert [b[1] for b in blocks[0:2 * NB:2]] == h_order

        def x_rows(i):
            return x[i * B:(i + 1) * B, :].rearrange("(k p) f -> p k f", p=P)

        def tiles(buf):
            return buf[:, :].rearrange("p (k f) -> p k f", f=P)

        def final(m):
            return jobs[m][0] == LAST

        def y_at(m):
            p, i = jobs[m][:2]
            return (y_hi[p % 2][:, i * B:(i + 1) * B], y_lo[p % 2][:, i * B:(i + 1) * B])

        def splits_before(m):
            return sum(not final(k) for k in range(m))

        @block.sync
        def _(sp):
            def load_weights():
                for s in range(2):
                    for n in range(3):
                        sp.dma_start(w_sb[s][n][:, :], weights[s][n]).then_inc(weights_landed, 16)
                    for n in range(2):
                        sp.dma_start(b_sb[s][n][:, :], biases[s][n].rearrange("(p a) -> p a", a=1))\
                            .then_inc(weights_landed, 16)
                    sp.dma_start(b3_sb[s][:, :], biases[s][2].partition_broadcast(P))\
                        .then_inc(weights_landed, 16)

            for t, (i, j, _, _) in enumerate(blocks):
                if t < NB:
                    sp.dma_start(tiles(partial[h_order[t]]), x_rows(h_order[t])).then_inc(x_landed[h_order[t]], 16)
                if t >= RAW:
                    sp.wait_ge(lo_ready, KT * (t - RAW + 1))
                sp.dma_start(raw[t % RAW][:, :], adj_blocks[i, j, :, :]).then_inc(raw_landed[t % RAW], 16)
                if t == NB:
                    load_weights()

        @block.gpsimd
        def _(pool):
            for n, j in enumerate(h_order):
                pool.wait_ge(rstd_ready, n + 1)
                if n:
                    pool.wait_ge(h_ready, n)
                for k in range(KT):
                    c = n * KT + k
                    ins = pool.tensor_scalar(yv[:, k * P:(k + 1) * P], partial[j][:, k * P:(k + 1) * P],
                                             rstd[:, c:c + 1], shift[:, c:c + 1], ALU.mult, ALU.add)
                ins.then_inc(scaled, 1)
                pool.wait_ge(scaled, n + 1)
                pool.tensor_scalar(yv[:, :], yv[:, :], 0.0, None, ALU.max).then_inc(relu_ready, 1)
                pool.wait_ge(y0_hi_ready, n + 1)
                at = slice(j * B, (j + 1) * B)
                pool.tensor_tensor(y_lo[0][:, at], yv[:, :], y_hi[0][:, at].bitcast(F32), ALU.subtract)\
                    .then_inc(h_ready, 1)

            ends = [m for m in range(len(jobs)) if final(m)]

            def store(m):
                i = jobs[m][1]
                pool.wait_ge(y_ready, m + 1)
                pool.dma_start(out[i * B:(i + 1) * B, :].rearrange("(k p) f -> p k f", p=P),
                               tiles(partial[i])).then_inc(out_written, 16)

            for n, m in enumerate(ends):
                i = jobs[m][1]
                pool.wait_ge(x0_ready, m + 1)
                pool.dma_start(tiles(partial[i]), x_rows(i)).then_inc(x_again[i], 16)
                if n:
                    store(ends[n - 1])
            store(ends[-1])
            pool.wait_ge(out_written, 16 * len(ends))

        @block.scalar
        def _(act):
            def root(n):
                act.wait_ge(var_ready, n + 1)
                at = slice(n * KT, (n + 1) * KT)
                act.activation(std[:, at], std[:, at], ACT.Sqrt).then_inc(std_ready, 1)

            def y0_hi(n):
                j = h_order[n]
                act.wait_ge(relu_ready, n + 1)
                act.activation(y_hi[0][:, j * B:(j + 1) * B], yv[:, :], ACT.Copy).then_inc(y0_hi_ready, 1)

            def split_hi(t, k):
                if t == 0 and k == 0:
                    root(0)
                    root(1)
                    y0_hi(0)
                if k == 0:
                    if before_in_slot[t] is not None:
                        act.wait_ge(products, last_use[before_in_slot[t]])
                    act.wait_ge(raw_landed[t % RAW], 16 * (t // RAW + 1))
                at = slice(k * B, (k + 1) * B)
                act.activation(a_hi[slot[t]][:, at], raw[t % RAW][:, at], ACT.Copy).then_inc(hi_ready, 1)
                n = t // 2
                if t % 2 == 0 and k == 3 and n + 2 < NB:
                    root(n + 2)
                if t % 2 == 1 and k == 1 and n + 1 < NB:
                    y0_hi(n + 1)

            for t in splits[-1]:
                for k in range(KT):
                    split_hi(t, k)

            tail = []
            for n, (kind, a) in enumerate(order):
                if kind in ("lead", "trail"):
                    for piece in tail:
                        split_hi(*piece)
                    pieces = [(t, k) for t in splits.get(n, []) for k in range(KT)]
                    now = len(pieces) if n + 1 == len(order) or order[n + 1][0] in ("lead", "trail") else AHEAD
                    for piece in pieces[:now]:
                        split_hi(*piece)
                    tail = pieces[now:]
                    continue
                m, s = a, 1 - jobs[a][0] % 2
                if kind == "layer1":
                    if m == 0:
                        act.wait_ge(weights_landed, 16 * 12)
                    act.wait_ge(layer_done[0], m + 1)
                    if m >= 1:
                        act.wait_ge(layer_done[1], m)
                    act.activation(h1[:, :], ps1[:, :], ACT.Identity, bias=b_sb[s][0][:, 0:1]).then_inc(bias1_done, 1)
                elif kind == "layer2":
                    act.wait_ge(layer_done[1], m + 1)
                    if m >= 1:
                        act.wait_ge(layer_done[2], m)
                    act.activation(h2[:, :], ps2[:, :], ACT.Identity, bias=b_sb[s][1][:, 0:1]).then_inc(bias2_done, 1)
                elif not final(m):
                    act.wait_ge(relu3_done, m + 1)
                    act.activation(y_at(m)[0], yv[:, :], ACT.Copy).then_inc(y_hi_ready, 1)

        @block.vector
        def _(dve):
            step = [0]

            def own(ins):
                step[0] += 1
                ins.then_inc(norm_step, 1)
                dve.wait_ge(norm_step, step[0])

            def leaky_relu(h):
                return dve.scalar_tensor_tensor(out=h[:, :], in0=h[:, :], scalar=SLOPE, in1=h[:, :],
                                                op0=ALU.mult, op1=ALU.max)

            def variance(n):
                j = h_order[n]
                dve.wait_ge(x_landed[j], 16)
                for k in range(KT):
                    ins = dve.bn_stats(stats[:, k, :], partial[j][:, k * P:(k + 1) * P])
                own(ins)
                for k in range(KT):
                    ins = dve.bn_aggr(moments[:, n * KT + k, :], stats[:, k, :])
                own(ins)
                at = slice(n * KT, (n + 1) * KT)
                dve.tensor_scalar(std[:, at], moments[:, at, 1], EPS, None, ALU.add).then_inc(var_ready, 1)

            def scale(n):
                at = slice(n * KT, (n + 1) * KT)
                dve.wait_ge(std_ready, n + 1)
                own(dve.reciprocal(rstd[:, at], std[:, at]))
                dve.scalar_tensor_tensor(out=shift[:, at], in0=moments[:, at, 0], scalar=-1.0,
                                         in1=rstd[:, at], op0=ALU.mult, op1=ALU.mult).then_inc(rstd_ready, 1)

            def split_lo(t, k):
                if t == 0 and k == 0:
                    for n in range(2):
                        variance(n)
                        scale(n)
                dve.wait_ge(hi_ready, KT * t + k + 1)
                at = slice(k * B, (k + 1) * B)
                dve.tensor_tensor(a_lo[slot[t]][:, at], raw[t % RAW][:, at],
                                  a_hi[slot[t]][:, at].bitcast(F32), ALU.subtract).then_inc(lo_ready, 1)
                n = t // 2
                if t % 2 == 0 and k == 1 and n + 2 < NB:
                    variance(n + 2)
                if t % 2 == 1 and k == 1 and n + 2 < NB:
                    scale(n + 2)

            for t in splits[-1]:
                for k in range(KT):
                    split_lo(t, k)

            tail = []
            for n, (kind, a) in enumerate(order):
                if kind in ("lead", "trail"):
                    t, e = a, (kind, a)
                    src = bank[kind][groups[row_of(kind, t)][0]]
                    for piece in tail:
                        split_lo(*piece)
                    if e in job_end:
                        m = job_end[e]
                        p, i = jobs[m][:2]
                        dve.wait_ge(products, product_no[e])
                        if m >= 1:
                            dve.wait_ge(layer_done[0], m)
                        if (p, i) in saved_as:
                            dve.wait_ge(saved, saved_as[(p, i)])
                            ins = dve.tensor_tensor(x0[:, :], src[:, :], partial[i][:, :], ALU.add)
                        else:
                            ins = dve.tensor_copy(x0[:, :], src[:, :])
                        ins.then_inc(x0_ready, 1)
                    elif e in save_no:
                        i = blocks[t][0]
                        dve.wait_ge(products, product_no[e])
                        dve.tensor_copy(partial[i][:, :], src[:, :]).then_inc(saved, 1)
                    pieces = [(t, k) for t in splits.get(n, []) for k in range(KT)]
                    now = len(pieces) if n + 1 == len(order) or order[n + 1][0] in ("lead", "trail") else AHEAD
                    for piece in pieces[:now]:
                        split_lo(*piece)
                    tail = pieces[now:]
                elif kind in ("layer1", "layer2"):
                    m = a
                    h, biased, ready = (h1, bias1_done, h1_ready) if kind == "layer1" else (h2, bias2_done, h2_ready)
                    dve.wait_ge(biased, m + 1)
                    leaky_relu(h).then_inc(ready, 1)
                elif kind == "layer3":
                    m = a
                    p, i = jobs[m][:2]
                    if m == 0:
                        dve.wait_ge(weights_landed, 16 * 12)
                    dve.wait_ge(layer_done[2], m + 1)
                    if m >= 1:
                        dve.wait_ge(y_ready, m)
                    dve.tensor_tensor(tiles(yv), tiles(ps3),
                                      b3_sb[1 - p % 2][:, :].unsqueeze(1).to_broadcast([P, KT, P]),
                                      ALU.add).then_inc(bias3_done, 1)
                    dve.wait_ge(bias3_done, m + 1)
                    leaky_relu(yv).then_inc(relu3_done, 1)
                    if final(m):
                        dve.wait_ge(relu3_done, m + 1)
                        dve.wait_ge(x_again[i], 16)
                        dve.tensor_tensor(partial[i][:, :], partial[i][:, :], yv[:, :], ALU.add)\
                            .then_inc(y_ready, 1)
                    else:
                        hi, lo = y_at(m)
                        dve.wait_ge(y_hi_ready, splits_before(m) + 1)
                        dve.tensor_tensor(lo, yv[:, :], hi.bitcast(F32), ALU.subtract).then_inc(y_ready, 1)

        @block.tensor
        def _(pe):
            for kind, a in order:
                if kind in ("lead", "trail"):
                    t, e = a, (kind, a)
                    i, j, p, q = blocks[t]
                    r = p if kind == "lead" else q
                    row = row_of(kind, t)
                    dst = bank[kind][groups[row][0]][:, :]
                    if r == 1:
                        pe.wait_ge(h_ready, h_order.index(j) + 1)
                    else:
                        pe.wait_ge(y_ready, job_of[(r - 1, j)] + 1)
                    if first[row] == e and groups[row][1]:
                        before = last[groups[row][1]]
                        if before in job_end:
                            pe.wait_ge(x0_ready, job_end[before] + 1)
                        else:
                            pe.wait_ge(saved, save_no[before])
                    for k in range(KT):
                        yk = slice((j * KT + k) * P, (j * KT + k + 1) * P)
                        ak = slice(k * B, (k + 1) * B)
                        yh, yl = y_hi[(r - 1) % 2][:, yk], y_lo[(r - 1) % 2][:, yk]
                        ah, al = a_hi[slot[t]][:, ak], a_lo[slot[t]][:, ak]
                        if kind == "lead":
                            pe.wait_ge(lo_ready, KT * t + k + 1)
                        pe.matmul(dst, yh, ah, start=(first[row] == e and k == 0), stop=False)
                        pe.matmul(dst, yh, al, start=False, stop=False)
                        ins = pe.matmul(dst, yl, ah, start=False, stop=(last[row] == e and k == KT - 1))
                    ins.then_inc(products, 1)
                    continue
                m, s = a, 1 - jobs[a][0] % 2
                w = w_sb[s][int(kind[-1]) - 1][:, :]
                if kind == "layer1":
                    if m == 0:
                        pe.wait_ge(weights_landed, 16 * 12)
                    pe.wait_ge(x0_ready, m + 1)
                    if m >= 1:
                        pe.wait_ge(h1_ready, m)
                    pe.matmul(ps1[:, :], w, x0[:, :], start=True, stop=True).then_inc(layer_done[0], 1)
                elif kind == "layer2":
                    pe.wait_ge(h1_ready, m + 1)
                    if m >= 1:
                        pe.wait_ge(h2_ready, m)
                    pe.matmul(ps2[:, :], w, h1[:, :], start=True, stop=True).then_inc(layer_done[1], 1)
                else:
                    pe.wait_ge(h2_ready, m + 1)
                    if m >= 1:
                        pe.wait_ge(bias3_done, m)
                    for k in range(KT):
                        ins = pe.matmul(ps3[:, k * P:(k + 1) * P], h2[:, k * P:(k + 1) * P], w,
                                        start=True, stop=True)
                    ins.then_inc(layer_done[2], 1)


def kernel(x, adj, L0_gnn_v_node_feats, L0_gnn_uv_W1, L0_gnn_uv_b1, L0_gnn_uv_W2, L0_gnn_uv_b2,
           L0_gnn_uv_W3, L0_gnn_uv_b3, L0_gnn_vu_W1, L0_gnn_vu_b1, L0_gnn_vu_W2, L0_gnn_vu_b2,
           L0_gnn_vu_W3, L0_gnn_vu_b3):
    import numpy as np
    import concourse.bacc as bacc
    from concourse.bass_utils import run_bass_kernel_spmd

    x = np.asarray(x)
    nb = x.shape[0] // B
    blocks = np.ascontiguousarray(np.asarray(adj).reshape(nb, B, nb, KT, P).transpose(0, 2, 4, 3, 1)
                                  .reshape(nb, nb, P, KT * B))
    arrays = {"x": x, "adj_blocks": blocks}
    for side, ws in (("uv", (L0_gnn_uv_W1, L0_gnn_uv_W2, L0_gnn_uv_W3)),
                     ("vu", (L0_gnn_vu_W1, L0_gnn_vu_W2, L0_gnn_vu_W3))):
        for n, w in enumerate(ws):
            arrays[f"{side}_w{n + 1}"] = np.asarray(w)
    for side, bs in (("uv", (L0_gnn_uv_b1, L0_gnn_uv_b2, L0_gnn_uv_b3)),
                     ("vu", (L0_gnn_vu_b1, L0_gnn_vu_b2, L0_gnn_vu_b3))):
        for n, b in enumerate(bs):
            arrays[f"{side}_b{n + 1}"] = np.asarray(b)
    nc = bacc.Bacc("TRN2", target_bir_lowering=False, num_devices=1)
    ap = {name: nc.dram_tensor(name, a.shape, mybir.dt.from_np(a.dtype), kind="ExternalInput").ap()
          for name, a in arrays.items()}
    out = nc.dram_tensor("out", x.shape, mybir.dt.from_np(x.dtype), kind="ExternalOutput").ap()
    build(nc, ap["x"], ap["adj_blocks"],
          [[ap[f"{side}_w{n + 1}"] for n in range(3)] for side in ("uv", "vu")],
          [[ap[f"{side}_b{n + 1}"] for n in range(3)] for side in ("uv", "vu")], out)
    return run_bass_kernel_spmd(nc, [arrays], core_ids=[0]).results[0]["out"]
```

```python
import concourse.bass as bass
from concourse import mybir
from contextlib import ExitStack

F32 = mybir.dt.float32
F32R = mybir.dt.float32r
ALU = mybir.AluOpType
ACT = mybir.ActivationFunctionType

P = 128
KT = 4
B = KT * P
RAW = 4
SPLIT = 5
LAG = 3
PARTS = 2
W = B // PARTS
AHEAD = 2
PRODUCT, LAYER = 2.6, 0.9
TO_LAYER1, TO_NEXT, TO_Y = 1.3, 3.0, 5.0
LOAD, SPLIT_TIME = 2.92, 2.6
EARLY = 0.5
START_UP = [(5, 6), (6, 7), (4, 5), (4, 6)]
START_DOWN = [(0, 0), (1, 0), (1, 1), (2, 1), (2, 0)]
LAST_ROWS = [3, 7, 0, 6, 1, 5, 2, 4]
SLOPE = 0.01
EPS = 1e-5
LAST = 5


def sweep_blocks(NB):
    def first_sweep(i):
        upper = [(i, j, 1, None) for j in range(i + 1, NB)]
        lower = [(i, j, 1, 2) for j in range(i)]
        row = []
        while upper or lower:
            if upper:
                row.append(upper.pop(0))
            if lower and (len(lower) > 1 or not upper):
                row.append(lower.pop(0))
        return row + [(i, i, 1, 2)]

    def start_with(sweep, first):
        at = {blk[:2]: blk for blk in sweep}
        return [at[k] for k in first] + [blk for blk in sweep if blk[:2] not in first]

    blocks = [(i, j, 1, None) for j in range(2, NB) for i in (0, 1)]
    blocks += [(0, 1, 1, None), (1, 1, 1, 2), (0, 0, 1, 2), (1, 0, 1, 2)]
    for i in range(2, NB):
        blocks += first_sweep(i)
    for p in (2, 4):
        up = [(i, j, p, p + 1) for i in range(NB - 2, -1, -1) for j in range(NB - 1, i, -1)]
        down = [(i, j, p + 1, p + 2) for i in range(NB) for j in range(i + 1)]
        up = start_with(up, START_UP)
        down = start_with(down, START_DOWN)
        if p + 1 == LAST:
            down = [(i, j, p + 1, None) for i in LAST_ROWS for j in range(i, -1, -1)]
        blocks += up + down
    return blocks


def plan(blocks, NB):
    need, rows = {}, {}
    for t, (i, j, p, q) in enumerate(blocks):
        for kind, r in (("lead", p), ("trail", q)):
            if r:
                need[(r, i)] = need.get((r, i), 0) + 1
                rows[(kind, r, i)] = rows.get((kind, r, i), 0) + 1
    known = {(0, j): 4.0 + 4.0 * ((j - 2) % NB) for j in range(NB)}
    order, jobs, waiting, splits = [], [], [], {}
    slot, ready, loaded = {}, {}, []
    groups, open_groups = {}, {"lead": [], "trail": []}
    bank_free = {"lead": [(0, None), (1, None)], "trail": [(0, None), (1, None)]}
    todo = {("lead", t) for t in range(len(blocks))} | {("trail", t) for t in range(len(blocks)) if blocks[t][3]}
    done = set()
    layer_done = [0, 0, 0]
    now = 0.0
    arriving = []

    def take_slot(k, at):
        t = len(slot)
        if t == len(blocks):
            return
        start = max(loaded[-1] if loaded else 2.0, ready[t - RAW] + 2.0 if t >= RAW else 0.0)
        loaded.append(start + LOAD)
        ready[t] = max(loaded[-1], at, ready[t - 1] if t else 0.0) + SPLIT_TIME
        slot[t] = k
        arriving.append((max(at, loaded[t]), t))

    def put_splits():
        while arriving and (arriving[0][0] <= now + EARLY or ready[arriving[0][1]] <= now + 0.1):
            splits.setdefault(len(order) - 1, []).append(arriving.pop(0)[1])

    def key_of(kind, t):
        i, _, p, q = blocks[t]
        return (kind, p if kind == "lead" else q, i)

    def when(kind, t):
        key = key_of(kind, t)
        y = (key[1] - 1, blocks[t][1])
        if t not in slot or ready[t] > now or y not in known or (kind == "trail" and ("lead", t) not in done):
            return None
        if key not in groups and not bank_free[kind]:
            return None
        if need[key[1:]] == 1 and len(jobs) > layer_done[0]:
            return None
        return max(known[y], ready[t])

    def product(kind, t):
        nonlocal now
        key = key_of(kind, t)
        if key not in groups:
            groups[key] = bank_free[kind].pop(0)
        put_splits()
        todo.discard((kind, t))
        done.add((kind, t))
        order.append((kind, t))
        now += PRODUCT
        rows[key] -= 1
        need[key[1:]] -= 1
        if rows[key] == 0:
            bank_free[kind].append((groups[key][0], key))
            if need[key[1:]] == 0:
                jobs.append((key[1], key[2], kind, t))
                waiting.append([now + TO_LAYER1, 1, len(jobs) - 1])
        if kind == "trail" or not blocks[t][3]:
            take_slot(slot[t], now)

    for k in range(SPLIT):
        take_slot(k, 0.0)
    while todo or waiting:
        able = [w for w in waiting if w[1] == 3 or layer_done[w[1]] >= w[2]]
        able = [w for w in able if layer_done[w[1] - 1] == w[2]]
        due = [w for w in able if w[0] <= now]
        if due:
            w = min(due, key=lambda w: w[2])
            waiting.remove(w)
            put_splits()
            now += LAYER
            order.append((f"layer{w[1]}", w[2]))
            layer_done[w[1] - 1] += 1
            if w[1] < 3:
                waiting.append([now + TO_NEXT, w[1] + 1, w[2]])
            else:
                known[jobs[w[2]][:2]] = now + TO_Y
            continue
        leads = [("lead", t) for t in range(len(blocks)) if ("lead", t) in todo and t in slot]
        trails = [("trail", t) for t in range(len(blocks)) if ("trail", t) in todo and ("lead", t) in done]
        times = {e: when(*e) for e in leads + trails}
        go_lead = [e for e in leads if times[e] is not None and times[e] <= now]
        go_trail = [e for e in trails if times[e] is not None and times[e] <= now]
        if go_trail and (not go_lead or len(trails) > LAG):
            product(*go_trail[0])
        elif go_lead:
            product(*go_lead[0])
        else:
            later = [t for t in list(times.values()) + [w[0] for w in able] if t is not None]
            now = max(now + 0.05, min([t for t in later if t > now] + [now + 0.2]))
    plan.time = now
    return order, jobs, splits, slot, groups


def build(nc, x, adj_blocks, weights, biases, out):
    NB = adj_blocks.shape[0]
    N = NB * B
    blocks = sweep_blocks(NB)
    order, jobs, splits, slot, groups = plan(blocks, NB)
    job_of = {(p, i): m for m, (p, i, _, _) in enumerate(jobs)}

    product_no, last_use = {}, {}
    for kind, a in order:
        if kind in ("lead", "trail"):
            product_no[(kind, a)] = len(product_no) + 1
            last_use[a] = product_no[(kind, a)]
    before_in_slot, holder = {}, {}
    for t in range(len(blocks)):
        before_in_slot[t] = holder.get(slot[t])
        holder[slot[t]] = t

    def row_of(kind, t):
        return (kind, blocks[t][2 if kind == "lead" else 3], blocks[t][0])

    first, last = {}, {}
    for e in product_no:
        first.setdefault(row_of(*e), e)
        last[row_of(*e)] = e
    job_end = {(kind, t): m for m, (_, _, kind, t) in enumerate(jobs)}
    saves = [e for e in product_no if last[row_of(*e)] == e and e not in job_end]
    save_no = {e: n + 1 for n, e in enumerate(saves)}
    saved_as = {row_of(*e)[1:]: n for e, n in save_no.items()}

    with ExitStack() as ctx:
        def sbuf(name, shape, dt=F32):
            return ctx.enter_context(nc.sbuf_tensor(name, shape, dt))

        def psum(name):
            return ctx.enter_context(nc.psum_tensor(name, [P, B], F32))

        def sem(name):
            return ctx.enter_context(nc.semaphore(name))

        raw = [sbuf(f"raw{k}", [P, KT * B]) for k in range(RAW)]
        a_hi = [sbuf(f"a_hi{k}", [P, KT * B], F32R) for k in range(SPLIT)]
        a_lo = [sbuf(f"a_lo{k}", [P, KT * B], F32R) for k in range(SPLIT)]
        y_hi = [sbuf(f"y_hi{g}", [P, N], F32R) for g in range(2)]
        y_lo = [sbuf(f"y_lo{g}", [P, N], F32R) for g in range(2)]
        partial = [sbuf(f"partial{i}", [P, B]) for i in range(NB)]
        x0 = sbuf("x0", [P, B])
        h1 = sbuf("h1", [P, B])
        h2 = sbuf("h2", [P, B])
        yv = sbuf("yv", [P, B])
        w_sb = [[sbuf(f"w{s}{n}", [P, P]) for n in range(3)] for s in range(2)]
        b_sb = [[sbuf(f"b{s}{n}", [P, 1]) for n in range(2)] for s in range(2)]
        b3_sb = [sbuf(f"b3_{s}", [P, P]) for s in range(2)]
        stats = sbuf("stats", [P, KT, 6])
        moments = sbuf("moments", [P, NB * KT, 2])
        std = sbuf("std", [P, NB * KT])
        rstd = sbuf("rstd", [P, NB * KT])
        shift = sbuf("shift", [P, NB * KT])

        bank = {"lead": [psum(f"lead{k}") for k in range(2)],
                "trail": [psum(f"trail{k}") for k in range(2)]}
        layer_bank = [[psum(f"layer{k}_{n}") for n in range(PARTS)] for k in range(2)]

        weights_landed = sem("weights_landed")
        x_landed = [sem(f"x_landed{j}") for j in range(NB)]
        raw_landed = [sem(f"raw_landed{k}") for k in range(RAW)]
        hi_ready = sem("hi_ready")
        lo_ready = sem("lo_ready")
        products = sem("products")
        saved = sem("saved")
        x0_ready = sem("x0_ready")
        layer_done = [sem(f"layer{n + 1}_done") for n in range(3)]
        bias1_done = sem("bias1_done")
        bias2_done = sem("bias2_done")
        h1_ready = sem("h1_ready")
        h2_ready = sem("h2_ready")
        bias3_done = sem("bias3_done")
        relu3_done = sem("relu3_done")
        y_hi_ready = sem("y_hi_ready")
        y_ready = sem("y_ready")
        norm_step = sem("norm_step")
        var_ready = sem("var_ready")
        std_ready = sem("std_ready")
        rstd_ready = sem("rstd_ready")
        scaled = sem("scaled")
        relu_ready = sem("relu_ready")
        y0_hi_ready = sem("y0_hi_ready")
        h_ready = sem("h_ready")
        x_again = [sem(f"x_again{i}") for i in range(NB)]
        out_written = sem("out_written")
        last_written = sem("last_written")

        block = ctx.enter_context(nc.Block())
        h_order = []
        for _, j, _, _ in blocks:
            if j not in h_order:
                h_order.append(j)
        assert [b[1] for b in blocks[0:2 * NB:2]] == h_order

        def x_rows(i):
            return x[i * B:(i + 1) * B, :].rearrange("(k p) f -> p k f", p=P)

        def tiles(buf, at=slice(0, B)):
            return buf[:, at].rearrange("p (k f) -> p k f", f=P)

        parts = [(n + 1, slice(n * W, (n + 1) * W)) for n in range(PARTS)]

        layer_events = [(int(kind[-1]), a) for kind, a in order if kind[:5] == "layer"]
        turn = {e: n for n, e in enumerate(layer_events)}

        def layer_out(layer, m, n):
            return layer_bank[turn[(layer, m)] % 2][n][:, 0:W]

        def final(m):
            return jobs[m][0] == LAST

        ends = [m for m in range(len(jobs)) if final(m)]

        def store(queue, m):
            i = jobs[m][1]
            queue.wait_ge(y_ready, PARTS * (m + 1))
            return queue.dma_start(out[i * B:(i + 1) * B, :].rearrange("(k p) f -> p k f", p=P),
                                   tiles(partial[i]))

        def y_at(m):
            p, i = jobs[m][:2]
            return (y_hi[p % 2][:, i * B:(i + 1) * B], y_lo[p % 2][:, i * B:(i + 1) * B])

        def splits_before(m):
            return sum(not final(k) for k in range(m))

        def pieces_now(n, pieces):
            if n + 1 == len(order) or order[n + 1][0] in ("lead", "trail"):
                return len(pieces)
            return AHEAD

        @block.sync
        def _(sp):
            def load_weights():
                for s in range(2):
                    for n in range(3):
                        sp.dma_start(w_sb[s][n][:, :], weights[s][n]).then_inc(weights_landed, 16)
                    for n in range(2):
                        sp.dma_start(b_sb[s][n][:, :], biases[s][n].rearrange("(p a) -> p a", a=1))\
                            .then_inc(weights_landed, 16)
                    sp.dma_start(b3_sb[s][:, :], biases[s][2].partition_broadcast(P))\
                        .then_inc(weights_landed, 16)

            for t, (i, j, _, _) in enumerate(blocks):
                if t < NB:
                    j0 = h_order[t]
                    sp.dma_start(tiles(partial[j0]), x_rows(j0)).then_inc(x_landed[j0], 16)
                if t >= RAW:
                    sp.wait_ge(lo_ready, KT * (t - RAW + 1))
                sp.dma_start(raw[t % RAW][:, :], adj_blocks[i, j, :, :]).then_inc(raw_landed[t % RAW], 16)
                if t == NB:
                    load_weights()
            store(sp, ends[-1]).then_inc(last_written, 16)
            sp.wait_ge(last_written, 16)

        @block.gpsimd
        def _(pool):
            for n, j in enumerate(h_order[1:], 1):
                pool.wait_ge(rstd_ready, n + 1)
                pool.wait_ge(h_ready, n)
                for k in range(KT):
                    c = n * KT + k
                    ins = pool.tensor_scalar(yv[:, k * P:(k + 1) * P], partial[j][:, k * P:(k + 1) * P],
                                             rstd[:, c:c + 1], shift[:, c:c + 1], ALU.mult, ALU.add)
                ins.then_inc(scaled, 1)
                pool.wait_ge(scaled, n)
                pool.tensor_scalar(yv[:, :], yv[:, :], 0.0, None, ALU.max).then_inc(relu_ready, 1)
                pool.wait_ge(y0_hi_ready, n + 1)
                at = slice(j * B, (j + 1) * B)
                pool.tensor_tensor(y_lo[0][:, at], yv[:, :], y_hi[0][:, at].bitcast(F32), ALU.subtract)\
                    .then_inc(h_ready, 1)

            for n, m in enumerate(ends):
                i = jobs[m][1]
                pool.wait_ge(x0_ready, PARTS * (m + 1))
                pool.dma_start(tiles(partial[i]), x_rows(i)).then_inc(x_again[i], 16)
                if n:
                    store(pool, ends[n - 1]).then_inc(out_written, 16)
            pool.wait_ge(out_written, 16 * (len(ends) - 1))

        @block.scalar
        def _(act):
            def root(n):
                act.wait_ge(var_ready, n + 1)
                at = slice(n * KT, (n + 1) * KT)
                act.activation(std[:, at], std[:, at], ACT.Sqrt).then_inc(std_ready, 1)

            def y0_hi(n):
                j = h_order[n]
                act.wait_ge(relu_ready, n + 1)
                act.activation(y_hi[0][:, j * B:(j + 1) * B], yv[:, :], ACT.Relu).then_inc(y0_hi_ready, 1)

            def split_hi(t, k):
                if t == 0 and k == 0:
                    root(0)
                    y0_hi(0)
                if k == 0:
                    if before_in_slot[t] is not None:
                        act.wait_ge(products, last_use[before_in_slot[t]])
                    act.wait_ge(raw_landed[t % RAW], 16 * (t // RAW + 1))
                at = slice(k * B, (k + 1) * B)
                act.activation(a_hi[slot[t]][:, at], raw[t % RAW][:, at], ACT.Copy).then_inc(hi_ready, 1)
                n = t // 2
                if (t, k) == (0, 2):
                    root(1)
                if (t, k) == (1, 3):
                    root(2)
                if t % 2 == 0 and t and k == 3 and n + 2 < NB:
                    root(n + 2)
                if t % 2 == 1 and k == 1 and n + 1 < NB:
                    y0_hi(n + 1)

            for t in splits[-1]:
                for k in range(KT):
                    split_hi(t, k)

            tail = []
            for n, (kind, a) in enumerate(order):
                m, s = a, 1 - jobs[a][0] % 2 if kind[:5] == "layer" else None
                if kind == "layer1":
                    if m == 0:
                        act.wait_ge(weights_landed, 16 * 12)
                    if m >= 1:
                        act.wait_ge(layer_done[1], PARTS * m)
                    for n1, at in parts:
                        act.wait_ge(layer_done[0], PARTS * m + n1)
                        act.activation(h1[:, at], layer_out(1, m, n1 - 1), ACT.Identity, bias=b_sb[s][0][:, 0:1])\
                            .then_inc(bias1_done, 1)
                elif kind == "layer2":
                    if m >= 1:
                        act.wait_ge(layer_done[2], PARTS * m)
                    for n1, at in parts:
                        act.wait_ge(layer_done[1], PARTS * m + n1)
                        act.activation(h2[:, at], layer_out(2, m, n1 - 1), ACT.Identity, bias=b_sb[s][1][:, 0:1])\
                            .then_inc(bias2_done, 1)
                elif kind == "layer3" and not final(m):
                    for n1, at in parts:
                        act.wait_ge(relu3_done, PARTS * m + n1)
                        act.activation(y_at(m)[0][:, at], yv[:, at], ACT.Copy).then_inc(y_hi_ready, 1)
                tail += [(t, k) for t in splits.get(n, []) for k in range(KT)]
                now = pieces_now(n, tail)
                for piece in tail[:now]:
                    split_hi(*piece)
                tail = tail[now:]

        @block.vector
        def _(dve):
            step = [0]

            def own(ins):
                step[0] += 1
                ins.then_inc(norm_step, 1)
                dve.wait_ge(norm_step, step[0])

            def leaky_relu(h, at):
                return dve.scalar_tensor_tensor(out=h[:, at], in0=h[:, at], scalar=SLOPE, in1=h[:, at],
                                                op0=ALU.mult, op1=ALU.max)

            def variance(n):
                j = h_order[n]
                dve.wait_ge(x_landed[j], 16)
                for k in range(KT):
                    ins = dve.bn_stats(stats[:, k, :], partial[j][:, k * P:(k + 1) * P])
                own(ins)
                for k in range(KT):
                    ins = dve.bn_aggr(moments[:, n * KT + k, :], stats[:, k, :])
                own(ins)
                at = slice(n * KT, (n + 1) * KT)
                dve.tensor_scalar(std[:, at], moments[:, at, 1], EPS, None, ALU.add).then_inc(var_ready, 1)

            def scale(n):
                at = slice(n * KT, (n + 1) * KT)
                dve.wait_ge(std_ready, n + 1)
                own(dve.reciprocal(rstd[:, at], std[:, at]))
                dve.scalar_tensor_tensor(out=shift[:, at], in0=moments[:, at, 0], scalar=-1.0,
                                         in1=rstd[:, at], op0=ALU.mult, op1=ALU.mult).then_inc(rstd_ready, 1)

            def first_y0():
                j = h_order[0]
                dve.wait_ge(rstd_ready, 1)
                for k in range(KT):
                    at = slice(k * P, (k + 1) * P)
                    ins = dve.tensor_scalar(yv[:, at], partial[j][:, at], rstd[:, k:k + 1], shift[:, k:k + 1],
                                            ALU.mult, ALU.add)
                ins.then_inc(relu_ready, 1)
                dve.wait_ge(y0_hi_ready, 1)
                at = slice(j * B, (j + 1) * B)
                dve.scalar_tensor_tensor(out=y_lo[0][:, at], in0=yv[:, :], scalar=0.0,
                                         in1=y_hi[0][:, at].bitcast(F32), op0=ALU.max, op1=ALU.subtract)\
                    .then_inc(h_ready, 1)

            def split_lo(t, k):
                if t == 0 and k == 0:
                    variance(0)
                    scale(0)
                    first_y0()
                dve.wait_ge(hi_ready, KT * t + k + 1)
                at = slice(k * B, (k + 1) * B)
                dve.tensor_tensor(a_lo[slot[t]][:, at], raw[t % RAW][:, at],
                                  a_hi[slot[t]][:, at].bitcast(F32), ALU.subtract).then_inc(lo_ready, 1)
                n = t // 2
                if (t, k) == (0, 0):
                    variance(1)
                if (t, k) == (0, 3):
                    scale(1)
                if (t, k) == (1, 1):
                    variance(2)
                if (t, k) == (2, 0):
                    scale(2)
                if t % 2 == 0 and t and k == 1 and n + 2 < NB:
                    variance(n + 2)
                if t % 2 == 1 and t > 1 and k == 1 and n + 2 < NB:
                    scale(n + 2)

            for t in splits[-1]:
                for k in range(KT):
                    split_lo(t, k)

            tail = []
            for n, (kind, a) in enumerate(order):
                if kind in ("lead", "trail"):
                    t, e = a, (kind, a)
                    src = bank[kind][groups[row_of(kind, t)][0]]
                    if e in job_end:
                        m = job_end[e]
                        p, i = jobs[m][:2]
                        dve.wait_ge(products, product_no[e])
                        if m >= 1:
                            dve.wait_ge(layer_done[0], PARTS * m)
                        if (p, i) in saved_as:
                            dve.wait_ge(saved, saved_as[(p, i)])
                        for _, at in parts:
                            if (p, i) in saved_as:
                                ins = dve.tensor_tensor(x0[:, at], src[:, at], partial[i][:, at], ALU.add)
                            else:
                                ins = dve.tensor_copy(x0[:, at], src[:, at])
                            ins.then_inc(x0_ready, 1)
                    elif e in save_no:
                        i = blocks[t][0]
                        dve.wait_ge(products, product_no[e])
                        dve.tensor_copy(partial[i][:, :], src[:, :]).then_inc(saved, 1)
                elif kind in ("layer1", "layer2"):
                    m = a
                    h, biased, ready = ((h1, bias1_done, h1_ready) if kind == "layer1"
                                        else (h2, bias2_done, h2_ready))
                    for n1, at in parts:
                        dve.wait_ge(biased, PARTS * m + n1)
                        leaky_relu(h, at).then_inc(ready, 1)
                elif kind == "layer3":
                    m = a
                    p, i = jobs[m][:2]
                    if m == 0:
                        dve.wait_ge(weights_landed, 16 * 12)
                    if m >= 1:
                        dve.wait_ge(y_ready, PARTS * m)
                    for n1, at in parts:
                        dve.wait_ge(layer_done[2], PARTS * m + n1)
                        dve.tensor_tensor(tiles(yv, at),
                                          layer_out(3, m, n1 - 1).rearrange("p (k f) -> p k f", f=P),
                                          b3_sb[1 - p % 2][:, :].unsqueeze(1).to_broadcast([P, W // P, P]),
                                          ALU.add).then_inc(bias3_done, 1)
                    for n1, at in parts:
                        dve.wait_ge(bias3_done, PARTS * m + n1)
                        leaky_relu(yv, at).then_inc(relu3_done, 1)
                    if final(m):
                        dve.wait_ge(x_again[i], 16)
                        for n1, at in parts:
                            dve.wait_ge(relu3_done, PARTS * m + n1)
                            dve.tensor_tensor(partial[i][:, at], partial[i][:, at], yv[:, at], ALU.add)\
                                .then_inc(y_ready, 1)
                    else:
                        hi, lo = y_at(m)
                        for n1, at in parts:
                            dve.wait_ge(y_hi_ready, PARTS * splits_before(m) + n1)
                            dve.tensor_tensor(lo[:, at], yv[:, at], hi[:, at].bitcast(F32), ALU.subtract)\
                                .then_inc(y_ready, 1)
                tail += [(t, k) for t in splits.get(n, []) for k in range(KT)]
                now = pieces_now(n, tail)
                for piece in tail[:now]:
                    split_lo(*piece)
                tail = tail[now:]

        @block.tensor
        def _(pe):
            for kind, a in order:
                if kind in ("lead", "trail"):
                    t, e = a, (kind, a)
                    i, j, p, q = blocks[t]
                    r = p if kind == "lead" else q
                    row = row_of(kind, t)
                    dst = bank[kind][groups[row][0]][:, :]
                    if r == 1:
                        pe.wait_ge(h_ready, h_order.index(j) + 1)
                    if first[row] == e and groups[row][1]:
                        before = last[groups[row][1]]
                        if before in job_end:
                            pe.wait_ge(x0_ready, PARTS * (job_end[before] + 1))
                        else:
                            pe.wait_ge(saved, save_no[before])
                    for k in range(KT):
                        yk = slice((j * KT + k) * P, (j * KT + k + 1) * P)
                        ak = slice(k * B, (k + 1) * B)
                        yh, yl = y_hi[(r - 1) % 2][:, yk], y_lo[(r - 1) % 2][:, yk]
                        ah, al = a_hi[slot[t]][:, ak], a_lo[slot[t]][:, ak]
                        if r > 1 and k % (W // P) == 0:
                            pe.wait_ge(y_ready, PARTS * job_of[(r - 1, j)] + k // (W // P) + 1)
                        if kind == "lead":
                            pe.wait_ge(lo_ready, KT * t + k + 1)
                        pe.matmul(dst, yh, ah, start=(first[row] == e and k == 0), stop=False)
                        pe.matmul(dst, yh, al, start=False, stop=False)
                        ins = pe.matmul(dst, yl, ah, start=False, stop=(last[row] == e and k == KT - 1))
                    ins.then_inc(products, 1)
                    continue
                m, s = a, 1 - jobs[a][0] % 2
                layer = int(kind[-1])
                w = w_sb[s][layer - 1][:, :]
                if m == 0 and layer == 1:
                    pe.wait_ge(weights_landed, 16 * 12)
                if turn[(layer, m)] >= 2:
                    before, b = layer_events[turn[(layer, m)] - 2]
                    pe.wait_ge((bias1_done, bias2_done, bias3_done)[before - 1], PARTS * (b + 1))
                for n1, at in parts:
                    dst = layer_out(layer, m, n1 - 1)
                    if layer == 1:
                        pe.wait_ge(x0_ready, PARTS * m + n1)
                        ins = pe.matmul(dst, w, x0[:, at], start=True, stop=True)
                    elif layer == 2:
                        pe.wait_ge(h1_ready, PARTS * m + n1)
                        ins = pe.matmul(dst, w, h1[:, at], start=True, stop=True)
                    else:
                        pe.wait_ge(h2_ready, PARTS * m + n1)
                        for k in range(0, W, P):
                            ins = pe.matmul(dst[:, k:k + P], h2[:, at.start + k:at.start + k + P], w,
                                            start=True, stop=True)
                    ins.then_inc(layer_done[layer - 1], 1)


def kernel(x, adj, L0_gnn_v_node_feats, L0_gnn_uv_W1, L0_gnn_uv_b1, L0_gnn_uv_W2, L0_gnn_uv_b2,
           L0_gnn_uv_W3, L0_gnn_uv_b3, L0_gnn_vu_W1, L0_gnn_vu_b1, L0_gnn_vu_W2, L0_gnn_vu_b2,
           L0_gnn_vu_W3, L0_gnn_vu_b3):
    import numpy as np
    import concourse.bacc as bacc
    from concourse.bass_utils import run_bass_kernel_spmd

    x = np.asarray(x)
    nb = x.shape[0] // B
    blocks = np.ascontiguousarray(np.asarray(adj).reshape(nb, B, nb, KT, P).transpose(0, 2, 4, 3, 1)
                                  .reshape(nb, nb, P, KT * B))
    arrays = {"x": x, "adj_blocks": blocks}
    for side, ws in (("uv", (L0_gnn_uv_W1, L0_gnn_uv_W2, L0_gnn_uv_W3)),
                     ("vu", (L0_gnn_vu_W1, L0_gnn_vu_W2, L0_gnn_vu_W3))):
        for n, w in enumerate(ws):
            arrays[f"{side}_w{n + 1}"] = np.asarray(w)
    for side, bs in (("uv", (L0_gnn_uv_b1, L0_gnn_uv_b2, L0_gnn_uv_b3)),
                     ("vu", (L0_gnn_vu_b1, L0_gnn_vu_b2, L0_gnn_vu_b3))):
        for n, b in enumerate(bs):
            arrays[f"{side}_b{n + 1}"] = np.asarray(b)
    nc = bacc.Bacc("TRN2", target_bir_lowering=False, num_devices=1)
    ap = {name: nc.dram_tensor(name, a.shape, mybir.dt.from_np(a.dtype), kind="ExternalInput").ap()
          for name, a in arrays.items()}
    out = nc.dram_tensor("out", x.shape, mybir.dt.from_np(x.dtype), kind="ExternalOutput").ap()
    build(nc, ap["x"], ap["adj_blocks"],
          [[ap[f"{side}_w{n + 1}"] for n in range(3)] for side in ("uv", "vu")],
          [[ap[f"{side}_b{n + 1}"] for n in range(3)] for side in ("uv", "vu")], out)
    return run_bass_kernel_spmd(nc, [arrays], core_ids=[0]).results[0]["out"]
```
